# Optimizing a Trainium2 kernel written in Bass

```python
import numpy as np
import jax
import jax.numpy as jnp

def _softmax(x, axis=-1):
    return jax.nn.softmax(x, axis=axis)

def _gelu(x):
    return jax.nn.gelu(x, approximate=True)

def _silu(x):
    return jax.nn.silu(x)

def _sigmoid(x):
    return jax.nn.sigmoid(x)

def _layernorm(x, axis=-1, eps=1e-05):
    m = jnp.mean(x, axis=axis, keepdims=True)
    v = jnp.var(x, axis=axis, keepdims=True)
    return (x - m) / jnp.sqrt(v + eps)

def _scatter_add(tgt, idx, src, axis=0):
    return tgt.at[idx].add(src)

def _segment_sum(src, seg, n):
    return jax.ops.segment_sum(src, seg, n)
kernel_name = 'mk_rec_standalone_d1_rec_r8_5958ae'

def setup_inputs(seed: int=0):
    np.random.seed(seed)
    _w = jnp.asarray

    def _rec_inputs():
        import jax
        import jax.numpy as jnp
        _rk = jax.random.key(seed)
        r_dense = -0.00338568 + 1.0005 * jax.random.normal(jax.random.fold_in(_rk, 1), (2048, 13), jnp.float32)
        r_sparse_idx = jnp.stack([jax.random.randint(jax.random.fold_in(jax.random.fold_in(_rk, 2), 0), (2048,), 2, 12500, jnp.int32), jax.random.randint(jax.random.fold_in(jax.random.fold_in(_rk, 2), 1), (2048,), 1, 99999, jnp.int32), jax.random.randint(jax.random.fold_in(jax.random.fold_in(_rk, 2), 2), (2048,), 0, 12500, jnp.int32), jax.random.randint(jax.random.fold_in(jax.random.fold_in(_rk, 2), 3), (2048,), 5, 12500, jnp.int32), jax.random.randint(jax.random.fold_in(jax.random.fold_in(_rk, 2), 4), (2048,), 20, 99993, jnp.int32), jax.random.randint(jax.random.fold_in(jax.random.fold_in(_rk, 2), 5), (2048,), 0, 99993, jnp.int32), jax.random.randint(jax.random.fold_in(jax.random.fold_in(_rk, 2), 6), (2048,), 2, 99999, jnp.int32), jax.random.randint(jax.random.fold_in(jax.random.fold_in(_rk, 2), 7), (2048,), 2, 99995, jnp.int32), jax.random.randint(jax.random.fold_in(jax.random.fold_in(_rk, 2), 8), (2048,), 0, 99999, jnp.int32), jax.random.randint(jax.random.fold_in(jax.random.fold_in(_rk, 2), 9), (2048,), 2, 99986, jnp.int32), jax.random.randint(jax.random.fold_in(jax.random.fold_in(_rk, 2), 10), (2048,), 4, 99999, jnp.int32), jax.random.randint(jax.random.fold_in(jax.random.fold_in(_rk, 2), 11), (2048,), 15, 99999, jnp.int32), jax.random.randint(jax.random.fold_in(jax.random.fold_in(_rk, 2), 12), (2048,), 0, 99989, jnp.int32), jax.random.randint(jax.random.fold_in(jax.random.fold_in(_rk, 2), 13), (2048,), 5, 99990, jnp.int32), jax.random.randint(jax.random.fold_in(jax.random.fold_in(_rk, 2), 14), (2048,), 2, 99996, jnp.int32), jax.random.randint(jax.random.fold_in(jax.random.fold_in(_rk, 2), 15), (2048,), 3, 99994, jnp.int32), jax.random.randint(jax.random.fold_in(jax.random.fold_in(_rk, 2), 16), (2048,), 0, 99998, jnp.int32), jax.random.randint(jax.random.fold_in(jax.random.fold_in(_rk, 2), 17), (2048,), 13, 99998, jnp.int32), jax.random.randint(jax.random.fold_in(jax.random.fold_in(_rk, 2), 18), (2048,), 10, 12498, jnp.int32), jax.random.randint(jax.random.fold_in(jax.random.fold_in(_rk, 2), 19), (2048,), 0, 99999, jnp.int32), jax.random.randint(jax.random.fold_in(jax.random.fold_in(_rk, 2), 20), (2048,), 0, 99995, jnp.int32), jax.random.randint(jax.random.fold_in(jax.random.fold_in(_rk, 2), 21), (2048,), 1, 99998, jnp.int32), jax.random.randint(jax.random.fold_in(jax.random.fold_in(_rk, 2), 22), (2048,), 1, 99997, jnp.int32), jax.random.randint(jax.random.fold_in(jax.random.fold_in(_rk, 2), 23), (2048,), 2, 99989, jnp.int32), jax.random.randint(jax.random.fold_in(jax.random.fold_in(_rk, 2), 24), (2048,), 6, 12500, jnp.int32), jax.random.randint(jax.random.fold_in(jax.random.fold_in(_rk, 2), 25), (2048,), 2, 99995, jnp.int32)], axis=1)
        return (r_dense, r_sparse_idx)
    r_dense, r_sparse_idx = _rec_inputs()

    def _L0_rec_setup():
        import jax, jax.numpy as jnp
        import numpy as np
        B, NF, D, V, NDENSE = (2048, 26, 64, 12500, 13)
        key = jax.random.key(seed)
        ks = jax.random.split(key, 16)
        s = 0.05
        return {'dense': jax.random.normal(ks[0], (B, NDENSE), jnp.float32), 'sparse_idx': jax.random.randint(ks[1], (B, NF), 0, V), 'emb_tables': jax.random.normal(ks[2], (NF, V, D), jnp.float32) * s, 'dw1': jax.random.normal(ks[3], (NDENSE, D), jnp.float32) * s, 'db1': jnp.zeros((D,), jnp.float32), 'dw2': jax.random.normal(ks[4], (D, D), jnp.float32) * s, 'db2': jnp.zeros((D,), jnp.float32), 'ow1': jax.random.normal(ks[5], ((NF + 1) * D + NF * (NF + 1) // 2, 512), jnp.float32) * s, 'ob1': jnp.zeros((512,), jnp.float32), 'ow2': jax.random.normal(ks[6], (512, 256), jnp.float32) * s, 'ob2': jnp.zeros((256,), jnp.float32), 'ow3': jax.random.normal(ks[7], (256, 128), jnp.float32) * s, 'ob3': jnp.zeros((128,), jnp.float32), 'ow4': jax.random.normal(ks[8], (128, 1), jnp.float32) * s, 'ob4': jnp.zeros((1,), jnp.float32)}
    _L0_rec_all = _L0_rec_setup()
    _L0_rec_in = {k: v for k, v in _L0_rec_all.items() if k in ('emb_tables', 'dw1', 'db1', 'dw2', 'db2', 'ow1', 'ob1', 'ow2', 'ob2', 'ow3', 'ob3', 'ow4', 'ob4')}
    del _L0_rec_all
    return {'r_dense': r_dense, 'r_sparse_idx': r_sparse_idx, 'L0_rec_emb_tables': _L0_rec_in['emb_tables'], 'L0_rec_dw1': _L0_rec_in['dw1'], 'L0_rec_db1': _L0_rec_in['db1'], 'L0_rec_dw2': _L0_rec_in['dw2'], 'L0_rec_db2': _L0_rec_in['db2'], 'L0_rec_ow1': _L0_rec_in['ow1'], 'L0_rec_ob1': _L0_rec_in['ob1'], 'L0_rec_ow2': _L0_rec_in['ow2'], 'L0_rec_ob2': _L0_rec_in['ob2'], 'L0_rec_ow3': _L0_rec_in['ow3'], 'L0_rec_ob3': _L0_rec_in['ob3'], 'L0_rec_ow4': _L0_rec_in['ow4'], 'L0_rec_ob4': _L0_rec_in['ob4']}

def reference(r_dense, r_sparse_idx, L0_rec_emb_tables, L0_rec_dw1, L0_rec_db1, L0_rec_dw2, L0_rec_db2, L0_rec_ow1, L0_rec_ob1, L0_rec_ow2, L0_rec_ob2, L0_rec_ow3, L0_rec_ob3, L0_rec_ow4, L0_rec_ob4):
    import jax
    import jax.numpy as jnp

    def _L0_rec_ref(dense, sparse_idx, emb_tables, dw1, db1, dw2, db2, ow1, ob1, ow2, ob2, ow3, ob3, ow4, ob4):
        import jax, jax.numpy as jnp
        import numpy as np
        B, NF, D, V, NDENSE = (2048, 26, 64, 12500, 13)
        h = jax.nn.relu(dense @ dw1 + db1)
        dense_emb = jax.nn.relu(h @ dw2 + db2)
        f_ids = jnp.arange(emb_tables.shape[0])[None, :]
        sparse_emb = emb_tables[f_ids, sparse_idx]
        emb = jnp.concatenate([dense_emb[:, None, :], sparse_emb], axis=1)
        inter = jnp.einsum('bfd,bgd->bfg', emb, emb)
        iu0, iu1 = jnp.triu_indices(emb.shape[1], k=1)
        pairs = inter[:, iu0, iu1]
        z = jnp.concatenate([emb.reshape(emb.shape[0], -1), pairs], axis=1)
        z = jax.nn.relu(z @ ow1 + ob1)
        z = jax.nn.relu(z @ ow2 + ob2)
        z = jax.nn.relu(z @ ow3 + ob3)
        return z @ ow4 + ob4
    y = _L0_rec_ref(r_dense, r_sparse_idx, L0_rec_emb_tables, L0_rec_dw1, L0_rec_db1, L0_rec_dw2, L0_rec_db2, L0_rec_ow1, L0_rec_ob1, L0_rec_ow2, L0_rec_ob2, L0_rec_ow3, L0_rec_ob3, L0_rec_ow4, L0_rec_ob4)
    return y

_drawn_inputs = setup_inputs


def setup_inputs(seed=0):
    import zlib

    import numpy as np

    out = dict(_drawn_inputs(seed))
    spreads = {'L0_rec_db1': (0.0, 0.1),
     'L0_rec_db2': (0.0, 0.1),
     'L0_rec_ob1': (0.0, 0.1),
     'L0_rec_ob2': (0.0, 0.1),
     'L0_rec_ob3': (0.0, 0.1)}
    factors = {}
    for name, (base, spread) in spreads.items():
        noise = np.random.default_rng([zlib.crc32(name.encode()), seed]).standard_normal(out[name].shape)
        drawn = base * np.exp(spread * noise) if base else spread * noise
        out[name] = jnp.asarray(drawn.astype(out[name].dtype))
    for name, factor in factors.items():
        out[name] = (out[name] * factor).astype(out[name].dtype)
    return out
```

```python
from contextlib import ExitStack

import numpy as np

import concourse.bass as bass
from concourse import mybir

F32 = mybir.dt.float32
I32 = mybir.dt.int32
U32 = mybir.dt.uint32
ALU = mybir.AluOpType
ACT = mybir.ActivationFunctionType

P = 128
TILES = 2
GROUPS = [(0, 4), (4, 8), (8, 12), (12, 13)]


def bass_dlrm_kernel(
    nc: bass.Bass,
    dense_t: bass.AP,
    idx: bass.AP,
    row_base: bass.AP,
    table: bass.AP,
    dw1: bass.AP,
    dw2: bass.AP,
    ow1: bass.AP,
    ow1_pairs: bass.AP,
    ow2: bass.AP,
    ow3: bass.AP,
    ow4: bass.AP,
    biases: bass.AP,
    ident: bass.AP,
    out: bass.AP,
    V: int,
):
    ND, B = dense_t.shape
    D = dw1.shape[1]
    H1, H2, H3 = ow1.shape[1], ow2.shape[1], ow3.shape[1]
    N = TILES * P
    MACROS = B // N
    NF = idx.shape[2] // TILES
    NP = NF // 2
    SLOTS = NF + 1
    NDELTA = (SLOTS - 1) // 2
    QUAD = 32
    PC = 3
    PR = SLOTS // PC * NDELTA
    M1, M2 = H1 // P, H2 // P
    CHUNK = 512
    COLS = TILES * NF
    assert SLOTS % PC == 0 and PR <= P and 2 * D == P and H3 == P and GROUPS[-1][1] == NP

    with ExitStack() as ctx:
        def sb(name, shape, dt=F32):
            return ctx.enter_context(nc.sbuf_tensor(name, shape, dt))

        def psum(name, shape):
            return ctx.enter_context(nc.psum_tensor(name, shape, F32))

        def sem(name):
            return ctx.enter_context(nc.semaphore(name))

        tr_ps = psum("tr_ps", [P, 2, CHUNK])
        l1_ps = psum("l1_ps", [P, 2, CHUNK])
        gram_ps = psum("gram_ps", [P, 2 * TILES, CHUNK])

        idx_raw = sb("idx_raw", [P, MACROS, COLS], I32)
        base_sb = sb("base_sb", [P, COLS], I32)
        wrap = sb("wrap", [P, MACROS, COLS])
        idx_f = sb("idx_f", [P, MACROS, COLS])
        all_rows = sb("all_rows", [P, (MACROS + 1) * COLS], U32)
        rows = sb("rows", [P, TILES, NF], U32)
        emb = sb("emb", [P, TILES, NP, 2 * D])
        feat = sb("feat", [P, QUAD, N])
        gram_b = sb("gram_b", [P, TILES, SLOTS + NDELTA, QUAD])
        pairs_b = sb("pairs_b", [P, TILES, SLOTS, NDELTA])
        pairs = sb("pairs", [PR, PC, N])
        dense_sb = sb("dense_sb", [ND, B])
        dense_h = sb("dense_h", [D, B])
        dense_e = sb("dense_e", [D, B])
        dw1_sb = sb("dw1_sb", [ND, D])
        dw2_sb = sb("dw2_sb", [D, D])
        w1_sb = sb("w1_sb", [P, NP, H1])
        w1d_sb = sb("w1d_sb", [D, H1])
        w1p_sb = sb("w1p_sb", [PR, PC, H1])
        w2_sb = sb("w2_sb", [P, M1, H2])
        w3_sb = sb("w3_sb", [P, M2, H3])
        w4_sb = sb("w4_sb", [P, 1])
        bias_sb = sb("bias_sb", [P, 10])
        ident_sb = sb("ident_sb", [P, P])
        h1 = sb("h1", [P, M1, N])
        h2 = sb("h2", [P, M2, N])
        h3 = sb("h3", [P, N])
        y = sb("y", [1, B])

        OB1, OB2, OB3 = 0, M1, M1 + M2
        DB1, DB2, OB4 = OB3 + 1, OB3 + 2, OB3 + 3

        idx_in = sem("idx_in")
        gather_turn = sem("gather_turn")
        gram_turn = sem("gram_turn")
        dense_w_in = sem("dense_w_in")
        ident_in = sem("ident_in")
        w1_in = [sem(f"w1_in{n}") for n in range(len(GROUPS))]
        w1x_in = sem("w1x_in")
        w234_in = sem("w234_in")
        gathered = [[sem(f"gathered{t}_{n}") for n in range(NP)] for t in range(TILES)]
        out_stored = sem("out_stored")
        idx_step = sem("idx_step")
        rows_done = sem("rows_done")
        rows_in = sem("rows_in")
        zeros_in = sem("zeros_in")
        gram_turned = sem("gram_turned")
        dve_evac = sem("dve_evac")
        h1_dve = sem("h1_dve")
        h2_dve = sem("h2_dve")
        h3_ready = sem("h3_ready")
        dense_h_ready = sem("dense_h_ready")
        dense_e_ready = sem("dense_e_ready")
        dense_in = sem("dense_in")
        act_evac = sem("act_evac")
        gram_ext = sem("gram_ext")
        pairs_picked = sem("pairs_picked")
        h1_act = sem("h1_act")
        h2_act = sem("h2_act")
        y_ready = sem("y_ready")
        dense1_done = sem("dense1_done")
        dense2_done = sem("dense2_done")
        transposed = sem("transposed")
        gram_done = sem("gram_done")
        pairs_done = sem("pairs_done")
        l1_done = sem("l1_done")
        l2_done = sem("l2_done")
        l3_done = sem("l3_done")
        l4_done = sem("l4_done")

        TR_A, TR_B = [1, 2, 3, 4], [5, 6, 7, 8]
        EV_A, EV_B = [1, 1, 2, 2], [3, 3, 5, 4]
        EV_PAIRS = [4, 5]
        TR_N, EV_N = 8, 5

        w1_dram = ow1[D:D + NP * P, :].rearrange("(k p) n -> p k n", p=P)

        block = ctx.enter_context(nc.Block())

        @block.sync
        def _(sp):
            sp.dma_start(idx_raw[:], idx).then_inc(idx_in, 16)
            sp.dma_start(base_sb[:], row_base).then_inc(idx_in, 16)
            sp.dma_start(ident_sb[:], ident).then_inc(ident_in, 16)
            for n, (a, b) in enumerate(GROUPS):
                sp.dma_start(w1_sb[:, a:b, :], w1_dram[:, a:b, :]).then_inc(w1_in[n], 16)
            sp.dma_start(w1d_sb[:], ow1[0:D, :]).then_inc(w1x_in, 16)
            sp.dma_start(w1p_sb[:], ow1_pairs.rearrange("(c r) n -> r c n", r=PR)).then_inc(w1x_in, 16)
            sp.dma_start(w2_sb[:], ow2.rearrange("(k p) n -> p k n", p=P)).then_inc(w234_in, 16)
            sp.dma_start(w3_sb[:], ow3.rearrange("(k p) n -> p k n", p=P)).then_inc(w234_in, 16)
            sp.dma_start(w4_sb[:], ow4).then_inc(w234_in, 16)
            sp.wait_ge(y_ready, MACROS)
            sp.dma_start(out.rearrange("b o -> o b"), y[:]).then_inc(out_stored, 16)
            sp.wait_ge(out_stored, 16)

        @block.gpsimd
        def _(pool):
            def gather(t):
                for k in range(NP):
                    for e in range(2):
                        c = 2 * k + e
                        pool.indirect_dma_start(
                            out=emb[:, t, k, e * D:(e + 1) * D], out_offset=None, in_=table,
                            in_offset=bass.IndirectOffsetOnAxis(ap=rows[:, t, c:c + 1], axis=0),
                        ).then_inc(gathered[t][k], 16)

            with pool.Fori(0, MACROS) as m:
                for t in range(TILES):
                    pool.wait_ge(rows_in, m * TILES + t + 1)
                    pool.sem_inc(gather_turn, 1)
                    gather(t)

        @block.vector
        def _(dve):
            def next_rows(m, t):
                nc.vector.tensor_copy(rows[:, t, :], all_rows[:, bass.ds(m * COLS + t * NF, NF)]).then_inc(rows_in, 1)

            dve.wait_ge(idx_in, 32)
            step = 0
            for a, b in ((0, 1), (1, MACROS)):
                r, w, f = idx_raw[:, a:b, :], wrap[:, a:b, :], idx_f[:, a:b, :]
                base = base_sb[:].rearrange("p (o c) -> p o c", o=1).to_broadcast([P, b - a, COLS])
                nc.vector.tensor_scalar(w, r, 0.0, float(V), ALU.is_lt, ALU.mult).then_inc(idx_step, 1)
                dve.wait_ge(idx_step, step + 1)
                nc.vector.tensor_tensor(f, r, w, ALU.add).then_inc(idx_step, 1)
                dve.wait_ge(idx_step, step + 2)
                nc.vector.tensor_scalar(w, f, 0.0, float(V - 1), ALU.max, ALU.min).then_inc(idx_step, 1)
                dve.wait_ge(idx_step, step + 3)
                nc.vector.tensor_tensor(all_rows[:, a * COLS:b * COLS].rearrange("p (m c) -> p m c", c=COLS),
                                        w, base, ALU.add).then_inc(rows_done, 1)
                step += 3
                if a == 0:
                    dve.wait_ge(rows_done, 1)
                    for t in range(TILES):
                        next_rows(0, t)
            nc.vector.memset(all_rows[:, MACROS * COLS:], 0).then_inc(rows_done, 1)
            nc.vector.memset(feat[0:D, SLOTS:QUAD, :], 0.0).then_inc(zeros_in, 1)

            def evac_features(m, t, n):
                a, b = GROUPS[n]
                cols = slice(t * P, (t + 1) * P)
                src = tr_ps[:, n % 2, 0:(b - a) * P].rearrange("p (k c) -> p k c", c=P)
                dve.wait_ge(transposed, m * TR_N + (TR_A, TR_B)[t][n])
                nc.vector.tensor_copy(feat[:, a:b, cols], src)
                nc.vector.tensor_copy(feat[0:D, NP + a:NP + b, cols], src[D:P]).then_inc(dve_evac, 1)

            def turn_gram(m, t):
                dve.wait_ge(gram_done, m * TILES + t + 1)
                src = gram_ps[:, 2 * t:2 * t + 2, :].rearrange("p k (j g) -> p g (k j)", g=QUAD)[:, 0:SLOTS, :]
                nc.vector.transpose(gram_b[:, t, 0:SLOTS, :], src).then_inc(gram_turned, 1)

            def small_layers(m):
                dve.wait_ge(l2_done, (m + 1) * M2)
                nc.vector.tensor_scalar(h2[:, 1, :], gram_ps[:, 1, 0:N], bias_sb[:, OB2 + 1:OB2 + 2], 0.0,
                                        ALU.add, ALU.max).then_inc(h2_dve, 1)
                dve.wait_ge(l3_done, m + 1)
                nc.vector.tensor_scalar(h3[:], gram_ps[:, 2, 0:N], bias_sb[:, OB3:OB3 + 1], 0.0,
                                        ALU.add, ALU.max).then_inc(h3_ready, 1)

            def body(m, before):
                evac_features(m, 0, 1)
                if before is not None:
                    small_layers(before)
                evac_features(m, 0, 3)
                next_rows(m + 1, 0)
                turn_gram(m, 0)
                evac_features(m, 1, 1)
                evac_features(m, 1, 3)
                next_rows(m + 1, 1)
                turn_gram(m, 1)
                dve.wait_ge(pairs_done, m * TILES + 2)
                nc.vector.tensor_copy(pairs[:, :, P:2 * P],
                                      tr_ps[0:PR, 1, 0:PC * P].rearrange("p (c b) -> p c b", b=P)).then_inc(dve_evac, 1)
                dve.wait_ge(l1_done, m * 2 + 2)
                for j in (2, 3):
                    last = nc.vector.tensor_scalar(h1[:, j, :], l1_ps[:, 1, (j - 2) * N:(j - 1) * N],
                                                   bias_sb[:, OB1 + j:OB1 + j + 1], 0.0, ALU.add, ALU.max)
                last.then_inc(h1_dve, 1)

            dve.wait_ge(dense_w_in, 4 * 16)
            dve.wait_ge(rows_done, 3)
            body(0, None)
            with dve.Fori(1, MACROS) as m:
                body(m, m - 1)
            small_layers(MACROS - 1)

        @block.scalar
        def _(act):
            act.dma_start(bias_sb[:], biases).then_inc(dense_w_in, 16)
            act.dma_start(dense_sb[:], dense_t).then_inc(dense_w_in, 16)
            act.dma_start(dw1_sb[:], dw1).then_inc(dense_w_in, 16)
            act.dma_start(dw2_sb[:], dw2).then_inc(dense_w_in, 16)
            act.wait_ge(dense_w_in, 4 * 16)
            for c in range(B // CHUNK):
                cols = slice(c * CHUNK, (c + 1) * CHUNK)
                act.wait_ge(dense1_done, c + 1)
                nc.scalar.activation(dense_h[:, cols], gram_ps[0:D, c, :], ACT.Relu,
                                     bias=bias_sb[0:D, DB1:DB1 + 1]).then_inc(dense_h_ready, 1)
            for c in range(B // CHUNK):
                cols = slice(c * CHUNK, (c + 1) * CHUNK)
                act.wait_ge(dense2_done, c + 1)
                nc.scalar.activation(dense_e[:, cols], gram_ps[0:D, c, :], ACT.Relu,
                                     bias=bias_sb[0:D, DB2:DB2 + 1]).then_inc(dense_e_ready, 1)
            act.wait_ge(dense_e_ready, B // CHUNK)

            def evac_features(m, t, n):
                a, b = GROUPS[n]
                cols = slice(t * P, (t + 1) * P)
                src = tr_ps[:, n % 2, 0:(b - a) * P].rearrange("p (k c) -> p k c", c=P)
                act.wait_ge(transposed, m * TR_N + (TR_A, TR_B)[t][n])
                nc.scalar.copy(feat[:, a:b, cols], src)
                nc.scalar.copy(feat[0:D, NP + a:NP + b, cols], src[D:P]).then_inc(act_evac, 1)

            def pick_pairs(m, t):
                act.wait_ge(gram_turned, m * TILES + t + 1)
                nc.scalar.copy(gram_b[:, t, SLOTS:SLOTS + NDELTA, SLOTS - NDELTA:SLOTS],
                               gram_b[:, t, 0:NDELTA, SLOTS - NDELTA:SLOTS]).then_inc(gram_ext, 1)
                act.wait_ge(gram_ext, m * TILES + t + 1)
                flat = gram_b[:, t, :, :].rearrange("p g f -> p (g f)")
                src = bass.AP(tensor=flat.tensor, offset=flat.offset + QUAD,
                              ap=[flat.ap[0], [QUAD + 1, SLOTS], [QUAD, NDELTA]])
                nc.scalar.copy(pairs_b[:, t, :, :], src).then_inc(pairs_picked, 1)

            def hidden2(m):
                act.wait_ge(l2_done, m * M2 + 1)
                nc.scalar.activation(h2[:, 0, :], gram_ps[:, 0, 0:N], ACT.Relu,
                                     bias=bias_sb[:, OB2:OB2 + 1]).then_inc(h2_act, 1)

            def result(m):
                act.wait_ge(l4_done, m + 1)
                nc.scalar.activation(y[0:1, bass.ds(m * N, N)], gram_ps[0:1, 3, 0:N], ACT.Identity,
                                     bias=bias_sb[0:1, OB4:OB4 + 1]).then_inc(y_ready, 1)

            def body(m, before):
                evac_features(m, 0, 0)
                nc.scalar.copy(feat[0:D, NF, :], dense_e[:, bass.ds(m * N, N)]).then_inc(dense_in, 1)
                if before is not None:
                    hidden2(before)
                evac_features(m, 0, 2)
                if before is not None:
                    result(before)
                pick_pairs(m, 0)
                evac_features(m, 1, 0)
                act.wait_ge(pairs_done, m * TILES + 1)
                nc.scalar.copy(pairs[:, :, 0:P],
                               tr_ps[0:PR, 0, 0:PC * P].rearrange("p (c b) -> p c b", b=P)).then_inc(act_evac, 1)
                evac_features(m, 1, 2)
                pick_pairs(m, 1)
                act.wait_ge(l1_done, m * 2 + 1)
                for j in (0, 1):
                    last = nc.scalar.activation(h1[:, j, :], l1_ps[:, 0, j * N:(j + 1) * N], ACT.Relu,
                                                bias=bias_sb[:, OB1 + j:OB1 + j + 1])
                last.then_inc(h1_act, 1)

            body(0, None)
            with act.Fori(1, MACROS) as m:
                body(m, m - 1)
            hidden2(MACROS - 1)
            result(MACROS - 1)

        @block.tensor
        def _(pe):
            pe.wait_ge(dense_w_in, 4 * 16)
            for c in range(B // CHUNK):
                nc.tensor.matmul(gram_ps[0:D, c, :], dw1_sb[:], dense_sb[:, c * CHUNK:(c + 1) * CHUNK],
                                 start=True, stop=True).then_inc(dense1_done, 1)
            for c in range(B // CHUNK):
                pe.wait_ge(dense_h_ready, c + 1)
                nc.tensor.matmul(gram_ps[0:D, c, :], dw2_sb[:], dense_h[:, c * CHUNK:(c + 1) * CHUNK],
                                 start=True, stop=True).then_inc(dense2_done, 1)
            pe.wait_ge(ident_in, 16)

            def transposes(m, t, n):
                evac = (act_evac, dve_evac)[n % 2]
                before = {(0, 0): 0, (0, 1): 0, (0, 2): EV_A[0], (0, 3): EV_A[1],
                          (1, 0): EV_A[2], (1, 1): EV_A[3], (1, 2): EV_PAIRS[0], (1, 3): EV_B[1]}[t, n]
                pe.wait_ge(evac, m * EV_N + before)
                a, b = GROUPS[n]
                for k in range(a, b):
                    pe.wait_ge(gathered[t][k], m * 32 + 32)
                    last = nc.tensor.transpose(tr_ps[:, n % 2, (k - a) * P:(k - a + 1) * P], emb[:, t, k, :],
                                               ident_sb[:])
                last.then_inc(transposed, 1)

            def layer1(w, x, first=False, last=False):
                for j in range(M1):
                    mm = nc.tensor.matmul(l1_ps[:, j // 2, (j % 2) * N:(j % 2 + 1) * N], w[:, j * P:(j + 1) * P], x,
                                          start=first and j % 2 == 0, stop=last, skip_group_check=True)
                    if last and j % 2 == 1:
                        mm.then_inc(l1_done, 1)

            def features1(m, n, skip=0, only=NP):
                a, b = GROUPS[n]
                pe.wait_ge((act_evac, dve_evac)[n % 2], m * EV_N + EV_B[n])
                for k in range(a + skip, min(a + only, b)):
                    layer1(w1_sb[:, k, :], feat[:, k, :], first=(k == 0))

            def gram(m, t):
                pe.sem_inc(gram_turn, 1)
                for j in range(QUAD):
                    for q in range(P // QUAD):
                        s = t * P + q * QUAD + j
                        c = j % 16 * QUAD
                        mm = nc.tensor.matmul(gram_ps[q * QUAD:(q + 1) * QUAD, 2 * t + j // 16, c:c + SLOTS],
                                              feat[0:D, :, s], feat[0:D, 0:SLOTS, s], start=True, stop=True)
                mm.then_inc(gram_done, 1)

            def turn_pairs(m, t):
                pe.wait_ge(pairs_picked, m * TILES + t + 1)
                pe.wait_ge((act_evac, dve_evac)[t], m * EV_N + EV_PAIRS[t] - 1)
                flat = pairs_b[:, t, :, :].rearrange("p f d -> p (f d)")
                for c in range(PC):
                    mm = nc.tensor.transpose(tr_ps[0:PR, t, c * P:(c + 1) * P], flat[:, c * PR:(c + 1) * PR],
                                             ident_sb[:])
                mm.then_inc(pairs_done, 1)

            def layer2(m):
                pe.wait_ge(h1_act, m + 1)
                pe.wait_ge(h1_dve, m + 1)
                for j in range(M2):
                    for k in range(M1):
                        mm = nc.tensor.matmul(gram_ps[:, j, 0:N], w2_sb[:, k, j * P:(j + 1) * P], h1[:, k, :],
                                              start=(k == 0), stop=(k == M1 - 1))
                    mm.then_inc(l2_done, 1)

            def layer3(m):
                pe.wait_ge(h2_act, m + 1)
                pe.wait_ge(h2_dve, m + 1)
                for k in range(M2):
                    mm = nc.tensor.matmul(gram_ps[:, 2, 0:N], w3_sb[:, k, :], h2[:, k, :],
                                          start=(k == 0), stop=(k == M2 - 1))
                mm.then_inc(l3_done, 1)

            def layer4(m):
                pe.wait_ge(h3_ready, m + 1)
                nc.tensor.matmul(gram_ps[0:1, 3, 0:N], w4_sb[:], h3[:], start=True, stop=True).then_inc(l4_done, 1)

            def body(m, before):
                transposes(m, 0, 0)
                transposes(m, 0, 1)
                if before is not None:
                    layer2(before)
                transposes(m, 0, 2)
                if before is not None:
                    layer3(before)
                transposes(m, 0, 3)
                if before is not None:
                    layer4(before)
                    pe.wait_ge(y_ready, m)
                pe.wait_ge(dense_in, m + 1)
                pe.wait_ge(act_evac, m * EV_N + EV_A[2])
                pe.wait_ge(dve_evac, m * EV_N + EV_A[3])
                gram(m, 0)
                transposes(m, 1, 0)
                transposes(m, 1, 1)
                pe.wait_ge(h1_act, m)
                pe.wait_ge(h1_dve, m)
                features1(m, 0)
                turn_pairs(m, 0)
                features1(m, 1)
                transposes(m, 1, 2)
                transposes(m, 1, 3)
                features1(m, 2, only=3)
                pe.wait_ge(dve_evac, m * EV_N + EV_B[3])
                gram(m, 1)
                features1(m, 2, skip=3)
                features1(m, 3)
                turn_pairs(m, 1)
                layer1(w1d_sb[:], feat[0:D, NF, :])
                pe.wait_ge(dve_evac, m * EV_N + EV_PAIRS[1])
                for c in range(PC):
                    layer1(w1p_sb[:, c, :], pairs[:, c, :], last=(c == PC - 1))

            pe.wait_ge(zeros_in, 1)
            for s in w1_in:
                pe.wait_ge(s, 16)
            pe.wait_ge(w1x_in, 32)
            pe.wait_ge(w234_in, 48)
            body(0, None)
            with pe.Fori(1, MACROS) as m:
                body(m, m - 1)
            layer2(MACROS - 1)
            layer3(MACROS - 1)
            layer4(MACROS - 1)


def pair_rows(slots, deltas, emb_of_slot):
    n = len(emb_of_slot)
    number = {}
    for f in range(n):
        for g in range(f + 1, n):
            number[f, g] = len(number)
    order = []
    for s in range(slots):
        for d in range(1, deltas + 1):
            f, g = emb_of_slot[s], emb_of_slot[(s + d) % slots]
            order.append(number[min(f, g), max(f, g)])
    return order


def kernel(**inputs):
    import numpy as _np
    import concourse.bacc as _bacc
    from concourse import mybir as _mybir
    from concourse.bass_utils import run_bass_kernel_spmd as _run

    x = {k.removeprefix("L0_rec_"): _np.asarray(v) for k, v in inputs.items()}
    NF, V, D = x["emb_tables"].shape
    B = x["r_dense"].shape[0]
    NP, SLOTS = NF // 2, NF + 1
    macros = B // (TILES * P)

    idx = x["r_sparse_idx"].reshape(macros, TILES, P, NF).transpose(2, 0, 1, 3).reshape(P, macros, TILES * NF)
    emb_of_slot = [2 * k + 1 for k in range(NP)] + [2 * k + 2 for k in range(NP)] + [0]
    ow1_pairs = x["ow1"][SLOTS * D:][_np.array(pair_rows(SLOTS, NF // 2, emb_of_slot))]
    biases = _np.zeros((P, 10), _np.float32)
    biases[:, 0:4] = x["ob1"].reshape(4, P).T
    biases[:, 4:6] = x["ob2"].reshape(2, P).T
    biases[:, 6] = x["ob3"]
    biases[0:D, 7] = x["db1"]
    biases[0:D, 8] = x["db2"]
    biases[0, 9] = x["ob4"][0]
    row_base = _np.tile(_np.arange(NF, dtype=_np.int32) * V, (P, TILES))

    arrays = {
        "dense_t_dram": x["r_dense"].T,
        "idx_dram": idx,
        "row_base_dram": row_base,
        "table_dram": x["emb_tables"].reshape(NF * V, D),
        "dw1_dram": x["dw1"],
        "dw2_dram": x["dw2"],
        "ow1_dram": x["ow1"],
        "ow1_pairs_dram": ow1_pairs,
        "ow2_dram": x["ow2"],
        "ow3_dram": x["ow3"],
        "ow4_dram": x["ow4"],
        "biases_dram": biases,
        "ident_dram": _np.eye(P, dtype=_np.float32),
    }
    arrays = {k: _np.ascontiguousarray(v) for k, v in arrays.items()}
    nc = _bacc.Bacc("TRN2", target_bir_lowering=False, num_devices=1)
    args = [nc.dram_tensor(k, a.shape, _mybir.dt.from_np(a.dtype), kind="ExternalInput").ap()
            for k, a in arrays.items()]
    args.append(nc.dram_tensor("out_dram", (B, 1), F32, kind="ExternalOutput").ap())
    bass_dlrm_kernel(nc, *args, V)
    r = _run(nc, [arrays], core_ids=[0])
    return r.results[0]["out_dram"]
```

```python
from contextlib import ExitStack

import numpy as np

import concourse.bass as bass
from concourse import mybir

F32 = mybir.dt.float32
I32 = mybir.dt.int32
U32 = mybir.dt.uint32
ALU = mybir.AluOpType
ACT = mybir.ActivationFunctionType

P = 128
TILES = 2
GRAM_PARTS = 8
GROUPS = [(0, 4), (4, 8), (8, 12), (12, 13)]


def bass_dlrm_kernel(
    nc: bass.Bass,
    dense_t: bass.AP,
    idx: bass.AP,
    row_base: bass.AP,
    table: bass.AP,
    dw1: bass.AP,
    dw2: bass.AP,
    ow1: bass.AP,
    ow1_pairs: bass.AP,
    ow2: bass.AP,
    ow3: bass.AP,
    ow4: bass.AP,
    biases: bass.AP,
    ident: bass.AP,
    out: bass.AP,
    V: int,
):
    ND, B = dense_t.shape
    D = dw1.shape[1]
    H1, H2, H3 = ow1.shape[1], ow2.shape[1], ow3.shape[1]
    N = TILES * P
    MACROS = B // N
    NF = idx.shape[2] // TILES
    NP = NF // 2
    SLOTS = NF + 1
    NDELTA = (SLOTS - 1) // 2
    QUAD = 32
    PC = 3
    PR = SLOTS // PC * NDELTA
    M1, M2 = H1 // P, H2 // P
    CHUNK = 512
    COLS = TILES * NF
    BANK_OUTS = [(0, 1), (2, 3)]
    assert SLOTS % PC == 0 and PR <= P and 2 * D == P and H3 == P and GROUPS[-1][1] == NP

    with ExitStack() as ctx:
        def sb(name, shape, dt=F32):
            return ctx.enter_context(nc.sbuf_tensor(name, shape, dt))

        def psum(name, shape):
            return ctx.enter_context(nc.psum_tensor(name, shape, F32))

        def sem(name):
            return ctx.enter_context(nc.semaphore(name))

        tr_ps = psum("tr_ps", [P, 2, CHUNK])
        l1_ps = psum("l1_ps", [P, 2, CHUNK])
        gram_ps = psum("gram_ps", [P, 2 * TILES, CHUNK])
        SMALL = 2

        idx_raw = sb("idx_raw", [P, MACROS, COLS], I32)
        base_sb = sb("base_sb", [P, COLS], I32)
        wrap = sb("wrap", [P, MACROS, COLS])
        idx_f = sb("idx_f", [P, MACROS, COLS])
        all_rows = sb("all_rows", [P, (MACROS + 1) * COLS], U32)
        rows = sb("rows", [P, TILES, NF], U32)
        emb = sb("emb", [P, TILES, NP, 2 * D])
        feat = sb("feat", [P, QUAD, N])
        gram_b = sb("gram_b", [P, TILES, SLOTS + NDELTA, QUAD])
        pairs_b = sb("pairs_b", [P, TILES, SLOTS, NDELTA])
        pairs = sb("pairs", [PR, PC, N])
        dense_sb = sb("dense_sb", [ND, B])
        dense_h = sb("dense_h", [D, B])
        dense_e = sb("dense_e", [D, B])
        dw1_sb = sb("dw1_sb", [ND, D])
        dw2_sb = sb("dw2_sb", [D, D])
        w1_sb = sb("w1_sb", [P, NP, H1])
        w1d_sb = sb("w1d_sb", [D, H1])
        w1p_sb = sb("w1p_sb", [PR, PC, H1])
        w2_sb = sb("w2_sb", [P, M1, H2])
        w3_sb = sb("w3_sb", [P, M2, H3])
        w4_sb = sb("w4_sb", [P, 1])
        bias_sb = sb("bias_sb", [P, 10])
        ident_sb = sb("ident_sb", [P, P])
        h1 = sb("h1", [P, M1, N])
        h2 = sb("h2", [P, M2, N])
        h3 = sb("h3", [P, N])
        y = sb("y", [1, B])

        OB1, OB2, OB3 = 0, M1, M1 + M2
        DB1, DB2, OB4 = OB3 + 1, OB3 + 2, OB3 + 3

        idx_in = sem("idx_in")
        gather_turn = sem("gather_turn")
        gram_turn = sem("gram_turn")
        dense_w_in = sem("dense_w_in")
        ident_in = sem("ident_in")
        w1_in = [sem(f"w1_in{n}") for n in range(len(GROUPS))]
        w1x_in = sem("w1x_in")
        w234_in = sem("w234_in")
        gathered = [[sem(f"gathered{t}_{n}") for n in range(NP)] for t in range(TILES)]
        out_stored = sem("out_stored")
        idx_step = sem("idx_step")
        rows_done = sem("rows_done")
        rows_in = sem("rows_in")
        zeros_in = sem("zeros_in")
        gram_turned = sem("gram_turned")
        dve_evac = sem("dve_evac")
        h1_dve = sem("h1_dve")
        h2_dve = sem("h2_dve")
        h3_ready = sem("h3_ready")
        dense_h_ready = sem("dense_h_ready")
        dense_e_ready = sem("dense_e_ready")
        dense_in = sem("dense_in")
        act_evac = sem("act_evac")
        gram_ext = sem("gram_ext")
        pairs_picked = sem("pairs_picked")
        h1_act = sem("h1_act")
        h2_act = sem("h2_act")
        y_ready = sem("y_ready")
        dense1_done = sem("dense1_done")
        dense2_done = sem("dense2_done")
        transposed = sem("transposed")
        gram_done = sem("gram_done")
        pairs_done = sem("pairs_done")
        l1_done = sem("l1_done")
        l2_done = sem("l2_done")
        l3_done = sem("l3_done")
        l4_done = sem("l4_done")

        TR_A, TR_B = [1, 2, 3, 4], [5, 6, 7, 8]
        EV_A, EV_B = [1, 1, 2, 2], [3, 3, 5, 4]
        EV_PAIRS = [4, 5]
        TR_N, EV_N = 8, 5

        w1_dram = ow1[D:D + NP * P, :].rearrange("(k p) n -> p k n", p=P)

        block = ctx.enter_context(nc.Block())

        @block.sync
        def _(sp):
            sp.dma_start(idx_raw[:], idx).then_inc(idx_in, 16)
            sp.dma_start(ident_sb[:], ident).then_inc(ident_in, 16)
            for n, (a, b) in enumerate(GROUPS):
                sp.dma_start(w1_sb[:, a:b, :], w1_dram[:, a:b, :]).then_inc(w1_in[n], 16)
            sp.dma_start(w1d_sb[:], ow1[0:D, :]).then_inc(w1x_in, 16)
            sp.dma_start(w1p_sb[:], ow1_pairs.rearrange("(c r) n -> r c n", r=PR)).then_inc(w1x_in, 16)
            sp.dma_start(w2_sb[:], ow2.rearrange("(k p) n -> p k n", p=P)).then_inc(w234_in, 16)
            sp.dma_start(w3_sb[:], ow3.rearrange("(k p) n -> p k n", p=P)).then_inc(w234_in, 16)
            sp.dma_start(w4_sb[:], ow4).then_inc(w234_in, 16)
            sp.wait_ge(y_ready, MACROS)
            sp.dma_start(out.rearrange("b o -> o b"), y[:]).then_inc(out_stored, 16)
            sp.wait_ge(out_stored, 16)

        @block.gpsimd
        def _(pool):
            def gather(t):
                for k in range(NP):
                    for e in range(2):
                        c = 2 * k + e
                        pool.indirect_dma_start(
                            out=emb[:, t, k, e * D:(e + 1) * D], out_offset=None, in_=table,
                            in_offset=bass.IndirectOffsetOnAxis(ap=rows[:, t, c:c + 1], axis=0),
                        ).then_inc(gathered[t][k], 16)

            with pool.Fori(0, MACROS) as m:
                for t in range(TILES):
                    pool.wait_ge(rows_in, m * TILES + t + 1)
                    pool.sem_inc(gather_turn, 1)
                    gather(t)

        @block.vector
        def _(dve):
            def next_rows(m, t):
                nc.vector.tensor_copy(rows[:, t, :], all_rows[:, bass.ds(m * COLS + t * NF, NF)]).then_inc(rows_in, 1)

            dve.wait_ge(idx_in, 32)
            step = 0
            for a, b in ((0, 1), (1, MACROS)):
                r, w, f = idx_raw[:, a:b, :], wrap[:, a:b, :], idx_f[:, a:b, :]
                base = base_sb[:].rearrange("p (o c) -> p o c", o=1).to_broadcast([P, b - a, COLS])
                nc.vector.tensor_scalar(w, r, 0.0, float(V), ALU.is_lt, ALU.mult).then_inc(idx_step, 1)
                dve.wait_ge(idx_step, step + 1)
                nc.vector.scalar_tensor_tensor(out=f, in0=r, scalar=float(-V), in1=w,
                                               op0=ALU.max, op1=ALU.add).then_inc(idx_step, 1)
                dve.wait_ge(idx_step, step + 2)
                if a == 0:
                    for t in range(TILES):
                        cols = slice(t * NF, (t + 1) * NF)
                        nc.vector.scalar_tensor_tensor(out=rows[:, t, :], in0=f[:, 0, cols], scalar=float(V - 1),
                                                       in1=base[:, 0, cols], op0=ALU.min,
                                                       op1=ALU.add).then_inc(rows_in, 1)
                else:
                    nc.vector.scalar_tensor_tensor(
                        out=all_rows[:, a * COLS:b * COLS].rearrange("p (m c) -> p m c", c=COLS), in0=f,
                        scalar=float(V - 1), in1=base, op0=ALU.min, op1=ALU.add).then_inc(rows_done, 1)
                step += 2
            nc.vector.memset(all_rows[:, MACROS * COLS:], 0).then_inc(rows_done, 1)
            nc.vector.memset(feat[0:D, SLOTS:QUAD, :], 0.0).then_inc(zeros_in, 1)

            def evac_features(m, t, n):
                a, b = GROUPS[n]
                cols = slice(t * P, (t + 1) * P)
                src = tr_ps[:, n % 2, 0:(b - a) * P].rearrange("p (k c) -> p k c", c=P)
                dve.wait_ge(transposed, m * TR_N + (TR_A, TR_B)[t][n])
                nc.vector.tensor_copy(feat[:, a:b, cols], src)
                nc.vector.tensor_copy(feat[0:D, NP + a:NP + b, cols], src[D:P]).then_inc(dve_evac, 1)

            def turn_gram(m, t):
                dve.wait_ge(gram_done, m * TILES + t + 1)
                src = gram_ps[:, 2 * t:2 * t + 2, :].rearrange("p k (j g) -> p g (k j)", g=QUAD)[:, 0:SLOTS, :]
                nc.vector.transpose(gram_b[:, t, 0:SLOTS, :], src).then_inc(gram_turned, 1)

            def small_layers(m):
                dve.wait_ge(l2_done, (m + 1) * M2)
                nc.vector.tensor_scalar(h2[:, 1, :], gram_ps[:, SMALL + 1, 0:N], bias_sb[:, OB2 + 1:OB2 + 2], 0.0,
                                        ALU.add, ALU.max).then_inc(h2_dve, 1)
                dve.wait_ge(l3_done, m + 1)
                nc.vector.tensor_scalar(h3[:], gram_ps[:, SMALL, 0:N], bias_sb[:, OB3:OB3 + 1], 0.0,
                                        ALU.add, ALU.max).then_inc(h3_ready, 1)

            def body(m, before):
                evac_features(m, 0, 1)
                evac_features(m, 0, 3)
                next_rows(m + 1, 0)
                if before is not None:
                    small_layers(before)
                turn_gram(m, 0)
                evac_features(m, 1, 1)
                evac_features(m, 1, 3)
                next_rows(m + 1, 1)
                turn_gram(m, 1)
                dve.wait_ge(pairs_done, m * TILES + 2)
                nc.vector.tensor_copy(pairs[:, :, P:2 * P],
                                      tr_ps[0:PR, 1, 0:PC * P].rearrange("p (c b) -> p c b", b=P)).then_inc(dve_evac, 1)
                dve.wait_ge(l1_done, m * 2 + 2)
                for j in (2, 3):
                    last = nc.vector.tensor_scalar(h1[:, j, :], l1_ps[:, 1, (j - 2) * N:(j - 1) * N],
                                                   bias_sb[:, OB1 + j:OB1 + j + 1], 0.0, ALU.add, ALU.max)
                last.then_inc(h1_dve, 1)

            dve.wait_ge(dense_w_in, 4 * 16)
            dve.wait_ge(rows_done, 2)
            body(0, None)
            with dve.Fori(1, MACROS) as m:
                body(m, m - 1)
            small_layers(MACROS - 1)

        @block.scalar
        def _(act):
            act.dma_start(base_sb[:], row_base).then_inc(idx_in, 16)
            act.dma_start(bias_sb[:], biases).then_inc(dense_w_in, 16)
            act.dma_start(dense_sb[:], dense_t).then_inc(dense_w_in, 16)
            act.dma_start(dw1_sb[:], dw1).then_inc(dense_w_in, 16)
            act.dma_start(dw2_sb[:], dw2).then_inc(dense_w_in, 16)
            act.wait_ge(dense_w_in, 4 * 16)
            for c in range(B // CHUNK):
                cols = slice(c * CHUNK, (c + 1) * CHUNK)
                act.wait_ge(dense1_done, c + 1)
                nc.scalar.activation(dense_h[:, cols], gram_ps[0:D, c, :], ACT.Relu,
                                     bias=bias_sb[0:D, DB1:DB1 + 1]).then_inc(dense_h_ready, 1)
            for c in range(B // CHUNK):
                cols = slice(c * CHUNK, (c + 1) * CHUNK)
                act.wait_ge(dense2_done, c + 1)
                nc.scalar.activation(dense_e[:, cols], gram_ps[0:D, c, :], ACT.Relu,
                                     bias=bias_sb[0:D, DB2:DB2 + 1]).then_inc(dense_e_ready, 1)
            act.wait_ge(dense_e_ready, B // CHUNK)

            def evac_features(m, t, n):
                a, b = GROUPS[n]
                cols = slice(t * P, (t + 1) * P)
                src = tr_ps[:, n % 2, 0:(b - a) * P].rearrange("p (k c) -> p k c", c=P)
                act.wait_ge(transposed, m * TR_N + (TR_A, TR_B)[t][n])
                nc.scalar.copy(feat[:, a:b, cols], src)
                nc.scalar.copy(feat[0:D, NP + a:NP + b, cols], src[D:P]).then_inc(act_evac, 1)

            def pick_pairs(m, t):
                act.wait_ge(gram_turned, m * TILES + t + 1)
                nc.scalar.copy(gram_b[:, t, SLOTS:SLOTS + NDELTA, SLOTS - NDELTA:SLOTS],
                               gram_b[:, t, 0:NDELTA, SLOTS - NDELTA:SLOTS]).then_inc(gram_ext, 1)
                act.wait_ge(gram_ext, m * TILES + t + 1)
                flat = gram_b[:, t, :, :].rearrange("p g f -> p (g f)")
                src = bass.AP(tensor=flat.tensor, offset=flat.offset + QUAD,
                              ap=[flat.ap[0], [QUAD + 1, SLOTS], [QUAD, NDELTA]])
                nc.scalar.copy(pairs_b[:, t, :, :], src).then_inc(pairs_picked, 1)

            def hidden2(m):
                act.wait_ge(l2_done, m * M2 + 1)
                nc.scalar.activation(h2[:, 0, :], gram_ps[:, SMALL, 0:N], ACT.Relu,
                                     bias=bias_sb[:, OB2:OB2 + 1]).then_inc(h2_act, 1)

            def result(m):
                act.wait_ge(l4_done, m + 1)
                nc.scalar.activation(y[0:1, bass.ds(m * N, N)], gram_ps[0:1, SMALL + 1, 0:N], ACT.Identity,
                                     bias=bias_sb[0:1, OB4:OB4 + 1]).then_inc(y_ready, 1)

            def body(m, before):
                evac_features(m, 0, 0)
                nc.scalar.copy(feat[0:D, NF, :], dense_e[:, bass.ds(m * N, N)]).then_inc(dense_in, 1)
                if before is not None:
                    hidden2(before)
                evac_features(m, 0, 2)
                if before is not None:
                    result(before)
                pick_pairs(m, 0)
                evac_features(m, 1, 0)
                act.wait_ge(pairs_done, m * TILES + 1)
                nc.scalar.copy(pairs[:, :, 0:P],
                               tr_ps[0:PR, 0, 0:PC * P].rearrange("p (c b) -> p c b", b=P)).then_inc(act_evac, 1)
                evac_features(m, 1, 2)
                pick_pairs(m, 1)
                act.wait_ge(l1_done, m * 2 + 1)
                for j in (0, 1):
                    last = nc.scalar.activation(h1[:, j, :], l1_ps[:, 0, j * N:(j + 1) * N], ACT.Relu,
                                                bias=bias_sb[:, OB1 + j:OB1 + j + 1])
                last.then_inc(h1_act, 1)

            body(0, None)
            with act.Fori(1, MACROS) as m:
                body(m, m - 1)
            hidden2(MACROS - 1)
            result(MACROS - 1)

        @block.tensor
        def _(pe):
            pe.wait_ge(dense_w_in, 4 * 16)
            for c in range(B // CHUNK):
                nc.tensor.matmul(gram_ps[0:D, c, :], dw1_sb[:], dense_sb[:, c * CHUNK:(c + 1) * CHUNK],
                                 start=True, stop=True).then_inc(dense1_done, 1)
            for c in range(B // CHUNK):
                pe.wait_ge(dense_h_ready, c + 1)
                nc.tensor.matmul(gram_ps[0:D, c, :], dw2_sb[:], dense_h[:, c * CHUNK:(c + 1) * CHUNK],
                                 start=True, stop=True).then_inc(dense2_done, 1)
            pe.wait_ge(ident_in, 16)

            def transposes(m, t, n):
                evac = (act_evac, dve_evac)[n % 2]
                before = {(0, 0): 0, (0, 1): 0, (0, 2): EV_A[0], (0, 3): EV_A[1],
                          (1, 0): EV_A[2], (1, 1): EV_A[3], (1, 2): EV_PAIRS[0], (1, 3): EV_B[1]}[t, n]
                pe.wait_ge(evac, m * EV_N + before)
                a, b = GROUPS[n]
                for k in range(a, b):
                    pe.wait_ge(gathered[t][k], m * 32 + 32)
                    last = nc.tensor.transpose(tr_ps[:, n % 2, (k - a) * P:(k - a + 1) * P], emb[:, t, k, :],
                                               ident_sb[:])
                last.then_inc(transposed, 1)

            def layer1(w, x, first=False, last=False, outs=range(M1)):
                for j in outs:
                    mm = nc.tensor.matmul(l1_ps[:, j // 2, (j % 2) * N:(j % 2 + 1) * N], w[:, j * P:(j + 1) * P], x,
                                          start=first and j % 2 == 0, stop=last, skip_group_check=True)
                    if last and j % 2 == 1:
                        mm.then_inc(l1_done, 1)

            def features1(m, a, b):
                for n, (ga, gb) in enumerate(GROUPS):
                    if max(a, ga) < min(b, gb):
                        pe.wait_ge((act_evac, dve_evac)[n % 2], m * EV_N + EV_B[n])
                    for k in range(max(a, ga), min(b, gb)):
                        layer1(w1_sb[:, k, :], feat[:, k, :])

            def gram_begins():
                pe.sem_inc(gram_turn, 1)

            def gram(t, part):
                n = QUAD // GRAM_PARTS
                for j in range(part * n, (part + 1) * n):
                    for q in range(P // QUAD):
                        s = t * P + q * QUAD + j
                        c = j % 16 * QUAD
                        mm = nc.tensor.matmul(gram_ps[q * QUAD:(q + 1) * QUAD, 2 * t + j // 16, c:c + SLOTS],
                                              feat[0:D, :, s], feat[0:D, 0:SLOTS, s], start=True, stop=True)
                if part == GRAM_PARTS - 1:
                    mm.then_inc(gram_done, 1)

            def turn_pairs(m, t):
                pe.wait_ge(pairs_picked, m * TILES + t + 1)
                pe.wait_ge((act_evac, dve_evac)[t], m * EV_N + EV_PAIRS[t] - 1)
                flat = pairs_b[:, t, :, :].rearrange("p f d -> p (f d)")
                for c in range(PC):
                    mm = nc.tensor.transpose(tr_ps[0:PR, t, c * P:(c + 1) * P], flat[:, c * PR:(c + 1) * PR],
                                             ident_sb[:])
                mm.then_inc(pairs_done, 1)

            def layer2(m, j):
                for k in range(M1):
                    if j == 0 and k in (0, 2):
                        pe.wait_ge((h1_act, h1_dve)[k // 2], m + 1)
                    mm = nc.tensor.matmul(gram_ps[:, SMALL + j, 0:N], w2_sb[:, k, j * P:(j + 1) * P], h1[:, k, :],
                                          start=(k == 0), stop=(k == M1 - 1))
                mm.then_inc(l2_done, 1)

            def layer3(m):
                for k in range(M2):
                    pe.wait_ge((h2_act, h2_dve)[k], m + 1)
                    mm = nc.tensor.matmul(gram_ps[:, SMALL, 0:N], w3_sb[:, k, :], h2[:, k, :],
                                          start=(k == 0), stop=(k == M2 - 1))
                mm.then_inc(l3_done, 1)

            def layer4(m):
                pe.wait_ge(h3_ready, m + 1)
                nc.tensor.matmul(gram_ps[0:1, SMALL + 1, 0:N], w4_sb[:], h3[:], start=True, stop=True).then_inc(l4_done, 1)

            def body(m, before):
                transposes(m, 0, 0)
                transposes(m, 0, 1)
                if before is not None:
                    layer2(before, 0)
                transposes(m, 0, 2)
                transposes(m, 0, 3)
                if before is not None:
                    layer2(before, 1)
                pe.wait_ge(dense_in, m + 1)
                pe.wait_ge(act_evac, m * EV_N + EV_A[2])
                pe.wait_ge(dve_evac, m * EV_N + EV_A[3])
                gram_begins()
                gram(0, 0)
                gram(0, 1)
                if before is not None:
                    layer3(before)
                gram(0, 2)
                gram(0, 3)
                if before is not None:
                    layer4(before)
                gram(0, 4)
                gram(0, 5)
                pe.wait_ge(h1_act, m)
                pe.wait_ge(h1_dve, m)
                layer1(w1d_sb[:], feat[0:D, NF, :], first=True, outs=BANK_OUTS[0])
                gram(0, 6)
                gram(0, 7)
                transposes(m, 1, 0)
                layer1(w1d_sb[:], feat[0:D, NF, :], first=True, outs=BANK_OUTS[1])
                features1(m, 0, 3)
                transposes(m, 1, 1)
                features1(m, 3, 4)
                turn_pairs(m, 0)
                features1(m, 4, 7)
                transposes(m, 1, 2)
                features1(m, 7, 9)
                transposes(m, 1, 3)
                features1(m, 9, 10)
                if before is not None:
                    pe.wait_ge(y_ready, m)
                pe.wait_ge(dve_evac, m * EV_N + EV_B[3])
                gram_begins()
                for n in range(GRAM_PARTS):
                    gram(1, n)
                    if n < M1:
                        layer1(w1_sb[:, 10, :], feat[:, 10, :], outs=[n])
                features1(m, 11, 12)
                turn_pairs(m, 1)
                features1(m, 12, 13)
                pe.wait_ge(dve_evac, m * EV_N + EV_PAIRS[1])
                for outs in BANK_OUTS:
                    for c in range(PC):
                        layer1(w1p_sb[:, c, :], pairs[:, c, :], last=(c == PC - 1), outs=outs)

            pe.wait_ge(zeros_in, 1)
            for s in w1_in:
                pe.wait_ge(s, 16)
            pe.wait_ge(w1x_in, 32)
            pe.wait_ge(w234_in, 48)
            body(0, None)
            with pe.Fori(1, MACROS) as m:
                body(m, m - 1)
            layer2(MACROS - 1, 0)
            layer2(MACROS - 1, 1)
            layer3(MACROS - 1)
            layer4(MACROS - 1)


def pair_rows(slots, deltas, emb_of_slot):
    n = len(emb_of_slot)
    number = {}
    for f in range(n):
        for g in range(f + 1, n):
            number[f, g] = len(number)
    order = []
    for s in range(slots):
        for d in range(1, deltas + 1):
            f, g = emb_of_slot[s], emb_of_slot[(s + d) % slots]
            order.append(number[min(f, g), max(f, g)])
    return order


def kernel(**inputs):
    import numpy as _np
    import concourse.bacc as _bacc
    from concourse import mybir as _mybir
    from concourse.bass_utils import run_bass_kernel_spmd as _run

    x = {k.removeprefix("L0_rec_"): _np.asarray(v) for k, v in inputs.items()}
    NF, V, D = x["emb_tables"].shape
    B = x["r_dense"].shape[0]
    NP, SLOTS = NF // 2, NF + 1
    macros = B // (TILES * P)

    idx = x["r_sparse_idx"].reshape(macros, TILES, P, NF).transpose(2, 0, 1, 3).reshape(P, macros, TILES * NF)
    emb_of_slot = [2 * k + 1 for k in range(NP)] + [2 * k + 2 for k in range(NP)] + [0]
    ow1_pairs = x["ow1"][SLOTS * D:][_np.array(pair_rows(SLOTS, NF // 2, emb_of_slot))]
    biases = _np.zeros((P, 10), _np.float32)
    biases[:, 0:4] = x["ob1"].reshape(4, P).T
    biases[:, 4:6] = x["ob2"].reshape(2, P).T
    biases[:, 6] = x["ob3"]
    biases[0:D, 7] = x["db1"]
    biases[0:D, 8] = x["db2"]
    biases[0, 9] = x["ob4"][0]
    row_base = _np.tile(_np.arange(NF, dtype=_np.int32) * V, (P, TILES))

    arrays = {
        "dense_t_dram": x["r_dense"].T,
        "idx_dram": idx,
        "row_base_dram": row_base,
        "table_dram": x["emb_tables"].reshape(NF * V, D),
        "dw1_dram": x["dw1"],
        "dw2_dram": x["dw2"],
        "ow1_dram": x["ow1"],
        "ow1_pairs_dram": ow1_pairs,
        "ow2_dram": x["ow2"],
        "ow3_dram": x["ow3"],
        "ow4_dram": x["ow4"],
        "biases_dram": biases,
        "ident_dram": _np.eye(P, dtype=_np.float32),
    }
    arrays = {k: _np.ascontiguousarray(v) for k, v in arrays.items()}
    nc = _bacc.Bacc("TRN2", target_bir_lowering=False, num_devices=1)
    args = [nc.dram_tensor(k, a.shape, _mybir.dt.from_np(a.dtype), kind="ExternalInput").ap()
            for k, a in arrays.items()]
    args.append(nc.dram_tensor("out_dram", (B, 1), F32, kind="ExternalOutput").ap())
    bass_dlrm_kernel(nc, *args, V)
    r = _run(nc, [arrays], core_ids=[0])
    return r.results[0]["out_dram"]
```

```python
from contextlib import ExitStack

import numpy as np

import concourse.bass as bass
from concourse import mybir

F32 = mybir.dt.float32
I32 = mybir.dt.int32
U32 = mybir.dt.uint32
ALU = mybir.AluOpType
ACT = mybir.ActivationFunctionType

P = 128
TILES = 2
GRAM_PARTS = 8
GROUPS = [(0, 4), (4, 8), (8, 12), (12, 13)]


def bass_dlrm_kernel(
    nc: bass.Bass,
    dense_t: bass.AP,
    idx: bass.AP,
    first: bass.AP,
    table: bass.AP,
    dw1: bass.AP,
    dw2: bass.AP,
    ow1: bass.AP,
    ow1_pairs: bass.AP,
    ow2: bass.AP,
    ow3: bass.AP,
    ow4: bass.AP,
    biases: bass.AP,
    ident: bass.AP,
    out: bass.AP,
    V: int,
):
    ND, B = dense_t.shape
    D = dw1.shape[1]
    H1, H2, H3 = ow1.shape[1], ow2.shape[1], ow3.shape[1]
    N = TILES * P
    MACROS = B // N
    NF = idx.shape[2] // TILES
    NP = NF // 2
    SLOTS = NF + 1
    NDELTA = (SLOTS - 1) // 2
    QUAD = 32
    PC = 3
    PR = SLOTS // PC * NDELTA
    M1, M2 = H1 // P, H2 // P
    CHUNK = 512
    COLS = TILES * NF
    BANK_OUTS = [(0, 1), (2, 3)]
    assert SLOTS % PC == 0 and PR <= P and 2 * D == P and H3 == P and GROUPS[-1][1] == NP

    with ExitStack() as ctx:
        def sb(name, shape, dt=F32):
            return ctx.enter_context(nc.sbuf_tensor(name, shape, dt))

        def psum(name, shape):
            return ctx.enter_context(nc.psum_tensor(name, shape, F32))

        def sem(name):
            return ctx.enter_context(nc.semaphore(name))

        tr_ps = psum("tr_ps", [P, 2, CHUNK])
        l1_ps = psum("l1_ps", [P, 2, CHUNK])
        gram_ps = psum("gram_ps", [P, 2 * TILES, CHUNK])
        SMALL = 2

        idx_raw = sb("idx_raw", [P, MACROS, COLS], I32)
        first_sb = sb("first_sb", [P, 2, COLS], I32)
        wrap = sb("wrap", [P, MACROS, COLS])
        idx_f = sb("idx_f", [P, MACROS, COLS])
        all_rows = sb("all_rows", [P, (MACROS + 1) * COLS], U32)
        rows = sb("rows", [P, TILES, NF], U32)
        emb = sb("emb", [P, TILES, NP, 2 * D])
        feat = sb("feat", [P, QUAD, N])
        gram_b = sb("gram_b", [P, TILES, SLOTS + NDELTA, QUAD])
        pairs_b = sb("pairs_b", [P, TILES, SLOTS, NDELTA])
        pairs = sb("pairs", [PR, PC, N])
        dense_sb = sb("dense_sb", [ND, B])
        dense_h = sb("dense_h", [D, B])
        dense_e = sb("dense_e", [D, B])
        dw1_sb = sb("dw1_sb", [ND, D])
        dw2_sb = sb("dw2_sb", [D, D])
        w1_sb = sb("w1_sb", [P, NP, H1])
        w1d_sb = sb("w1d_sb", [D, H1])
        w1p_sb = sb("w1p_sb", [PR, PC, H1])
        w2_sb = sb("w2_sb", [P, M1, H2])
        w3_sb = sb("w3_sb", [P, M2, H3])
        w4_sb = sb("w4_sb", [P, 1])
        bias_sb = sb("bias_sb", [P, 10])
        ident_sb = sb("ident_sb", [P, P])
        h1 = sb("h1", [P, M1, N])
        h2 = sb("h2", [P, M2, N])
        h3 = sb("h3", [P, N])
        y = sb("y", [1, B])

        OB1, OB2, OB3 = 0, M1, M1 + M2
        DB1, DB2, OB4 = OB3 + 1, OB3 + 2, OB3 + 3

        first_in = sem("first_in")
        idx_in = sem("idx_in")
        gather_turn = sem("gather_turn")
        gram_turn = sem("gram_turn")
        dense_w_in = sem("dense_w_in")
        ident_in = sem("ident_in")
        w1_in = [sem(f"w1_in{n}") for n in range(len(GROUPS))]
        w1x_in = sem("w1x_in")
        w234_in = sem("w234_in")
        gathered = [[sem(f"gathered{t}_{n}") for n in range(NP)] for t in range(TILES)]
        out_stored = sem("out_stored")
        idx_step = sem("idx_step")
        rows_done = sem("rows_done")
        rows_in = sem("rows_in")
        zeros_in = sem("zeros_in")
        gram_turned = sem("gram_turned")
        dve_evac = sem("dve_evac")
        h1_dve = sem("h1_dve")
        h2_dve = sem("h2_dve")
        h3_ready = sem("h3_ready")
        dense_h_ready = sem("dense_h_ready")
        dense_e_ready = sem("dense_e_ready")
        dense_in = sem("dense_in")
        act_evac = sem("act_evac")
        gram_ext = sem("gram_ext")
        pairs_picked = sem("pairs_picked")
        h1_act = sem("h1_act")
        h2_act = sem("h2_act")
        y_ready = sem("y_ready")
        dense1_done = sem("dense1_done")
        dense2_done = sem("dense2_done")
        transposed = sem("transposed")
        gram_done = sem("gram_done")
        pairs_done = sem("pairs_done")
        l1_done = sem("l1_done")
        l2_done = sem("l2_done")
        l3_done = sem("l3_done")
        l4_done = sem("l4_done")

        TR_A, TR_B = [1, 2, 3, 4], [5, 6, 7, 8]
        EV_A, EV_B = [1, 1, 2, 2], [3, 3, 5, 4]
        EV_PAIRS = [4, 5]
        TR_N, EV_N = 8, 5

        w1_dram = ow1[D:D + NP * P, :].rearrange("(k p) n -> p k n", p=P)

        block = ctx.enter_context(nc.Block())

        @block.sync
        def _(sp):
            sp.dma_start(first_sb[:], first).then_inc(first_in, 16)
            sp.dma_start(ident_sb[:], ident).then_inc(ident_in, 16)
            for n, (a, b) in enumerate(GROUPS):
                sp.dma_start(w1_sb[:, a:b, :], w1_dram[:, a:b, :]).then_inc(w1_in[n], 16)
            sp.dma_start(w1d_sb[:], ow1[0:D, :]).then_inc(w1x_in, 16)
            sp.dma_start(w1p_sb[:], ow1_pairs.rearrange("(c r) n -> r c n", r=PR)).then_inc(w1x_in, 16)
            sp.dma_start(w2_sb[:], ow2.rearrange("(k p) n -> p k n", p=P)).then_inc(w234_in, 16)
            sp.dma_start(w3_sb[:], ow3.rearrange("(k p) n -> p k n", p=P)).then_inc(w234_in, 16)
            sp.dma_start(w4_sb[:], ow4).then_inc(w234_in, 16)
            sp.wait_ge(y_ready, MACROS)
            sp.dma_start(out.rearrange("b o -> o b"), y[:]).then_inc(out_stored, 16)
            sp.wait_ge(out_stored, 16)

        @block.gpsimd
        def _(pool):
            def gather(t):
                for k in range(NP):
                    for e in range(2):
                        c = 2 * k + e
                        pool.indirect_dma_start(
                            out=emb[:, t, k, e * D:(e + 1) * D], out_offset=None, in_=table,
                            in_offset=bass.IndirectOffsetOnAxis(ap=rows[:, t, c:c + 1], axis=0),
                        ).then_inc(gathered[t][k], 16)

            with pool.Fori(0, MACROS) as m:
                for t in range(TILES):
                    pool.wait_ge(rows_in, m * TILES + t + 1)
                    pool.sem_inc(gather_turn, 1)
                    gather(t)

        @block.vector
        def _(dve):
            def next_rows(m, t):
                nc.vector.tensor_copy(rows[:, t, :], all_rows[:, bass.ds(m * COLS + t * NF, NF)]).then_inc(rows_in, 1)

            step = 0
            for a, b in ((0, 1), (1, MACROS)):
                if a == 0:
                    dve.wait_ge(first_in, 16)
                    r = first_sb[:, 1:2, :]
                else:
                    dve.wait_ge(idx_in, 16)
                    r = idx_raw[:, a:b, :]
                w, f = wrap[:, a:b, :], idx_f[:, a:b, :]
                base = first_sb[:, 0:1, :].to_broadcast([P, b - a, COLS])
                nc.vector.tensor_scalar(w, r, 0.0, float(V), ALU.is_lt, ALU.mult).then_inc(idx_step, 1)
                dve.wait_ge(idx_step, step + 1)
                nc.vector.scalar_tensor_tensor(out=f, in0=r, scalar=float(-V), in1=w,
                                               op0=ALU.max, op1=ALU.add).then_inc(idx_step, 1)
                dve.wait_ge(idx_step, step + 2)
                if a == 0:
                    for t in range(TILES):
                        cols = slice(t * NF, (t + 1) * NF)
                        nc.vector.scalar_tensor_tensor(out=rows[:, t, :], in0=f[:, 0, cols], scalar=float(V - 1),
                                                       in1=base[:, 0, cols], op0=ALU.min,
                                                       op1=ALU.add).then_inc(rows_in, 1)
                else:
                    nc.vector.scalar_tensor_tensor(
                        out=all_rows[:, a * COLS:b * COLS].rearrange("p (m c) -> p m c", c=COLS), in0=f,
                        scalar=float(V - 1), in1=base, op0=ALU.min, op1=ALU.add).then_inc(rows_done, 1)
                step += 2
            nc.vector.memset(all_rows[:, MACROS * COLS:], 0).then_inc(rows_done, 1)
            nc.vector.memset(feat[0:D, SLOTS:QUAD, :], 0.0).then_inc(zeros_in, 1)

            def evac_features(m, t, n):
                a, b = GROUPS[n]
                cols = slice(t * P, (t + 1) * P)
                src = tr_ps[:, n % 2, 0:(b - a) * P].rearrange("p (k c) -> p k c", c=P)
                dve.wait_ge(transposed, m * TR_N + (TR_A, TR_B)[t][n])
                nc.vector.tensor_copy(feat[:, a:b, cols], src)
                nc.vector.tensor_copy(feat[0:D, NP + a:NP + b, cols], src[D:P]).then_inc(dve_evac, 1)

            def turn_gram(m, t):
                dve.wait_ge(gram_done, m * TILES + t + 1)
                src = gram_ps[:, 2 * t:2 * t + 2, :].rearrange("p k (j g) -> p g (k j)", g=QUAD)[:, 0:SLOTS, :]
                nc.vector.transpose(gram_b[:, t, 0:SLOTS, :], src).then_inc(gram_turned, 1)

            def hidden2(m):
                dve.wait_ge(l2_done, (m + 1) * M2)
                nc.vector.tensor_scalar(h2[:, 1, :], gram_ps[:, SMALL + 1, 0:N], bias_sb[:, OB2 + 1:OB2 + 2], 0.0,
                                        ALU.add, ALU.max).then_inc(h2_dve, 1)

            def hidden3(m):
                dve.wait_ge(l3_done, m + 1)
                nc.vector.tensor_scalar(h3[:], gram_ps[:, SMALL, 0:N], bias_sb[:, OB3:OB3 + 1], 0.0,
                                        ALU.add, ALU.max).then_inc(h3_ready, 1)

            def body(m, before):
                evac_features(m, 0, 1)
                if before is not None:
                    hidden2(before)
                evac_features(m, 0, 3)
                if before is not None:
                    hidden3(before)
                next_rows(m + 1, 0)
                turn_gram(m, 0)
                evac_features(m, 1, 1)
                evac_features(m, 1, 3)
                next_rows(m + 1, 1)
                turn_gram(m, 1)
                dve.wait_ge(pairs_done, m * TILES + 2)
                nc.vector.tensor_copy(pairs[:, :, P:2 * P],
                                      tr_ps[0:PR, 1, 0:PC * P].rearrange("p (c b) -> p c b", b=P)).then_inc(dve_evac, 1)
                dve.wait_ge(l1_done, m * 2 + 2)
                for j in (2, 3):
                    last = nc.vector.tensor_scalar(h1[:, j, :], l1_ps[:, 1, (j - 2) * N:(j - 1) * N],
                                                   bias_sb[:, OB1 + j:OB1 + j + 1], 0.0, ALU.add, ALU.max)
                last.then_inc(h1_dve, 1)

            dve.wait_ge(dense_w_in, 4 * 16)
            dve.wait_ge(rows_done, 2)
            body(0, None)
            with dve.Fori(1, MACROS) as m:
                body(m, m - 1)
            hidden2(MACROS - 1)
            hidden3(MACROS - 1)

        @block.scalar
        def _(act):
            act.dma_start(idx_raw[:], idx).then_inc(idx_in, 16)
            act.dma_start(bias_sb[:], biases).then_inc(dense_w_in, 16)
            act.dma_start(dense_sb[:], dense_t).then_inc(dense_w_in, 16)
            act.dma_start(dw1_sb[:], dw1).then_inc(dense_w_in, 16)
            act.dma_start(dw2_sb[:], dw2).then_inc(dense_w_in, 16)
            act.wait_ge(dense_w_in, 4 * 16)
            for c in range(B // CHUNK):
                cols = slice(c * CHUNK, (c + 1) * CHUNK)
                act.wait_ge(dense1_done, c + 1)
                nc.scalar.activation(dense_h[:, cols], gram_ps[0:D, c, :], ACT.Relu,
                                     bias=bias_sb[0:D, DB1:DB1 + 1]).then_inc(dense_h_ready, 1)
            for c in range(B // CHUNK):
                cols = slice(c * CHUNK, (c + 1) * CHUNK)
                act.wait_ge(dense2_done, c + 1)
                nc.scalar.activation(dense_e[:, cols], gram_ps[0:D, c, :], ACT.Relu,
                                     bias=bias_sb[0:D, DB2:DB2 + 1]).then_inc(dense_e_ready, 1)
            act.wait_ge(dense_e_ready, B // CHUNK)

            def evac_features(m, t, n):
                a, b = GROUPS[n]
                cols = slice(t * P, (t + 1) * P)
                src = tr_ps[:, n % 2, 0:(b - a) * P].rearrange("p (k c) -> p k c", c=P)
                act.wait_ge(transposed, m * TR_N + (TR_A, TR_B)[t][n])
                nc.scalar.copy(feat[:, a:b, cols], src)
                nc.scalar.copy(feat[0:D, NP + a:NP + b, cols], src[D:P]).then_inc(act_evac, 1)

            def pick_pairs(m, t):
                act.wait_ge(gram_turned, m * TILES + t + 1)
                nc.scalar.copy(gram_b[:, t, SLOTS:SLOTS + NDELTA, SLOTS - NDELTA:SLOTS],
                               gram_b[:, t, 0:NDELTA, SLOTS - NDELTA:SLOTS]).then_inc(gram_ext, 1)
                act.wait_ge(gram_ext, m * TILES + t + 1)
                flat = gram_b[:, t, :, :].rearrange("p g f -> p (g f)")
                src = bass.AP(tensor=flat.tensor, offset=flat.offset + QUAD,
                              ap=[flat.ap[0], [QUAD + 1, SLOTS], [QUAD, NDELTA]])
                nc.scalar.copy(pairs_b[:, t, :, :], src).then_inc(pairs_picked, 1)

            def hidden2(m):
                act.wait_ge(l2_done, m * M2 + 1)
                nc.scalar.activation(h2[:, 0, :], gram_ps[:, SMALL, 0:N], ACT.Relu,
                                     bias=bias_sb[:, OB2:OB2 + 1]).then_inc(h2_act, 1)

            def result(m):
                act.wait_ge(l4_done, m + 1)
                nc.scalar.activation(y[0:1, bass.ds(m * N, N)], gram_ps[0:1, SMALL + 1, 0:N], ACT.Identity,
                                     bias=bias_sb[0:1, OB4:OB4 + 1]).then_inc(y_ready, 1)

            def body(m, before):
                evac_features(m, 0, 0)
                nc.scalar.copy(feat[0:D, NF, :], dense_e[:, bass.ds(m * N, N)]).then_inc(dense_in, 1)
                if before is not None:
                    hidden2(before)
                evac_features(m, 0, 2)
                if before is not None:
                    result(before)
                evac_features(m, 1, 0)
                pick_pairs(m, 0)
                act.wait_ge(pairs_done, m * TILES + 1)
                nc.scalar.copy(pairs[:, :, 0:P],
                               tr_ps[0:PR, 0, 0:PC * P].rearrange("p (c b) -> p c b", b=P)).then_inc(act_evac, 1)
                evac_features(m, 1, 2)
                pick_pairs(m, 1)
                act.wait_ge(l1_done, m * 2 + 1)
                for j in (0, 1):
                    last = nc.scalar.activation(h1[:, j, :], l1_ps[:, 0, j * N:(j + 1) * N], ACT.Relu,
                                                bias=bias_sb[:, OB1 + j:OB1 + j + 1])
                last.then_inc(h1_act, 1)

            body(0, None)
            with act.Fori(1, MACROS) as m:
                body(m, m - 1)
            hidden2(MACROS - 1)
            result(MACROS - 1)

        @block.tensor
        def _(pe):
            pe.wait_ge(dense_w_in, 4 * 16)
            for c in range(B // CHUNK):
                nc.tensor.matmul(gram_ps[0:D, c, :], dw1_sb[:], dense_sb[:, c * CHUNK:(c + 1) * CHUNK],
                                 start=True, stop=True).then_inc(dense1_done, 1)
            for c in range(B // CHUNK):
                pe.wait_ge(dense_h_ready, c + 1)
                nc.tensor.matmul(gram_ps[0:D, c, :], dw2_sb[:], dense_h[:, c * CHUNK:(c + 1) * CHUNK],
                                 start=True, stop=True).then_inc(dense2_done, 1)
            pe.wait_ge(ident_in, 16)

            def transposes(m, t, n):
                evac = (act_evac, dve_evac)[n % 2]
                before = {(0, 0): 0, (0, 1): 0, (0, 2): EV_A[0], (0, 3): EV_A[1],
                          (1, 0): EV_A[2], (1, 1): EV_A[3], (1, 2): EV_PAIRS[0], (1, 3): EV_B[1]}[t, n]
                pe.wait_ge(evac, m * EV_N + before)
                a, b = GROUPS[n]
                for k in range(a, b):
                    pe.wait_ge(gathered[t][k], m * 32 + 32)
                    last = nc.tensor.transpose(tr_ps[:, n % 2, (k - a) * P:(k - a + 1) * P], emb[:, t, k, :],
                                               ident_sb[:])
                last.then_inc(transposed, 1)

            def layer1(w, x, outs=range(M1), tiles=range(TILES), first=False, last=False):
                lo, n = tiles[0] * P, len(tiles) * P
                for j in outs:
                    c = j % 2 * N + lo
                    mm = nc.tensor.matmul(l1_ps[:, j // 2, c:c + n], w[:, j * P:(j + 1) * P], x[:, lo:lo + n],
                                          start=first and j % 2 == 0, stop=last, skip_group_check=True)
                    if last and j % 2 == 1:
                        mm.then_inc(l1_done, 1)

            def features1(k, outs=range(M1), tiles=range(TILES)):
                layer1(w1_sb[:, k, :], feat[:, k, :], outs, tiles)

            def features_in(m, t, n):
                pe.wait_ge((act_evac, dve_evac)[n % 2], m * EV_N + (EV_A, EV_B)[t][n])

            def gram_begins():
                pe.sem_inc(gram_turn, 1)

            def gram(t, part):
                n = QUAD // GRAM_PARTS
                for j in range(part * n, (part + 1) * n):
                    for q in range(P // QUAD):
                        s = t * P + q * QUAD + j
                        c = j % 16 * QUAD
                        mm = nc.tensor.matmul(gram_ps[q * QUAD:(q + 1) * QUAD, 2 * t + j // 16, c:c + SLOTS],
                                              feat[0:D, :, s], feat[0:D, 0:SLOTS, s], start=True, stop=True)
                if part == GRAM_PARTS - 1:
                    mm.then_inc(gram_done, 1)

            def turn_pairs(m, t):
                pe.wait_ge(pairs_picked, m * TILES + t + 1)
                pe.wait_ge((act_evac, dve_evac)[t], m * EV_N + EV_PAIRS[t] - 1)
                flat = pairs_b[:, t, :, :].rearrange("p f d -> p (f d)")
                for c in range(PC):
                    mm = nc.tensor.transpose(tr_ps[0:PR, t, c * P:(c + 1) * P], flat[:, c * PR:(c + 1) * PR],
                                             ident_sb[:])
                mm.then_inc(pairs_done, 1)

            def layer2(m, j):
                for k in range(M1):
                    if j == 0 and k in (0, 2):
                        pe.wait_ge((h1_act, h1_dve)[k // 2], m + 1)
                    mm = nc.tensor.matmul(gram_ps[:, SMALL + j, 0:N], w2_sb[:, k, j * P:(j + 1) * P], h1[:, k, :],
                                          start=(k == 0), stop=(k == M1 - 1))
                mm.then_inc(l2_done, 1)

            def layer3(m):
                for k in range(M2):
                    pe.wait_ge((h2_act, h2_dve)[k], m + 1)
                    mm = nc.tensor.matmul(gram_ps[:, SMALL, 0:N], w3_sb[:, k, :], h2[:, k, :],
                                          start=(k == 0), stop=(k == M2 - 1))
                mm.then_inc(l3_done, 1)

            def layer4(m):
                pe.wait_ge(h3_ready, m + 1)
                nc.tensor.matmul(gram_ps[0:1, SMALL + 1, 0:N], w4_sb[:], h3[:], start=True, stop=True).then_inc(l4_done, 1)

            def body(m, before):
                transposes(m, 0, 0)
                transposes(m, 0, 1)
                if before is not None:
                    layer2(before, 0)
                    layer2(before, 1)
                pe.wait_ge(h1_act, m)
                pe.wait_ge(h1_dve, m)
                pe.wait_ge(dense_in, m + 1)
                layer1(w1d_sb[:], feat[0:D, NF, :], first=True)
                features_in(m, 0, 0)
                for k in (0, 1):
                    features1(k, tiles=[0])
                transposes(m, 0, 2)
                if before is not None:
                    layer3(before)
                transposes(m, 0, 3)
                features1(2, tiles=[0])
                for n in (1, 2, 3):
                    features_in(m, 0, n)
                gram_begins()
                gram(0, 0)
                features1(3, BANK_OUTS[0], tiles=[0])
                gram(0, 1)
                if before is not None:
                    layer4(before)
                gram(0, 2)
                features1(3, BANK_OUTS[1], tiles=[0])
                gram(0, 3)
                features1(4, BANK_OUTS[0], tiles=[0])
                gram(0, 4)
                features1(4, BANK_OUTS[1], tiles=[0])
                gram(0, 5)
                features1(5, BANK_OUTS[0], tiles=[0])
                transposes(m, 1, 0)
                gram(0, 6)
                features1(5, BANK_OUTS[1], tiles=[0])
                gram(0, 7)
                features_in(m, 1, 0)
                for k in (0, 1):
                    features1(k, tiles=[1])
                for k in (6, 7, 8):
                    features1(k, tiles=[0])
                transposes(m, 1, 1)
                for k in (2, 3):
                    features1(k, tiles=[1])
                turn_pairs(m, 0)
                features_in(m, 1, 1)
                for k in (4, 5, 6):
                    features1(k, tiles=[1])
                pe.wait_ge(act_evac, m * EV_N + EV_PAIRS[0])
                for c in range(PC):
                    layer1(w1p_sb[:, c, :], pairs[:, c, :], tiles=[0])
                transposes(m, 1, 2)
                features1(7, tiles=[1])
                features1(9, tiles=[0])
                transposes(m, 1, 3)
                features_in(m, 1, 2)
                features1(8, tiles=[1])
                if before is not None:
                    pe.wait_ge(y_ready, m)
                features_in(m, 1, 3)
                gram_begins()
                for n in range(GRAM_PARTS):
                    gram(1, n)
                    if n < 2:
                        features1(9, BANK_OUTS[n], tiles=[1])
                    elif n < 2 + M1:
                        features1(10, [n - 2])
                features1(11)
                features1(12, [0])
                turn_pairs(m, 1)
                features1(12, [1, 2, 3])
                pe.wait_ge(dve_evac, m * EV_N + EV_PAIRS[1])
                for outs in BANK_OUTS:
                    for c in range(PC):
                        layer1(w1p_sb[:, c, :], pairs[:, c, :], outs, [1], last=(c == PC - 1))

            pe.wait_ge(zeros_in, 1)
            for s in w1_in:
                pe.wait_ge(s, 16)
            pe.wait_ge(w1x_in, 32)
            pe.wait_ge(w234_in, 48)
            body(0, None)
            with pe.Fori(1, MACROS) as m:
                body(m, m - 1)
            layer2(MACROS - 1, 0)
            layer2(MACROS - 1, 1)
            layer3(MACROS - 1)
            layer4(MACROS - 1)


def pair_rows(slots, deltas, emb_of_slot):
    n = len(emb_of_slot)
    number = {}
    for f in range(n):
        for g in range(f + 1, n):
            number[f, g] = len(number)
    order = []
    for s in range(slots):
        for d in range(1, deltas + 1):
            f, g = emb_of_slot[s], emb_of_slot[(s + d) % slots]
            order.append(number[min(f, g), max(f, g)])
    return order


def kernel(**inputs):
    import numpy as _np
    import concourse.bacc as _bacc
    from concourse import mybir as _mybir
    from concourse.bass_utils import run_bass_kernel_spmd as _run

    x = {k.removeprefix("L0_rec_"): _np.asarray(v) for k, v in inputs.items()}
    NF, V, D = x["emb_tables"].shape
    B = x["r_dense"].shape[0]
    NP, SLOTS = NF // 2, NF + 1
    macros = B // (TILES * P)

    idx = x["r_sparse_idx"].reshape(macros, TILES, P, NF).transpose(2, 0, 1, 3).reshape(P, macros, TILES * NF)
    emb_of_slot = [2 * k + 1 for k in range(NP)] + [2 * k + 2 for k in range(NP)] + [0]
    ow1_pairs = x["ow1"][SLOTS * D:][_np.array(pair_rows(SLOTS, NF // 2, emb_of_slot))]
    biases = _np.zeros((P, 10), _np.float32)
    biases[:, 0:4] = x["ob1"].reshape(4, P).T
    biases[:, 4:6] = x["ob2"].reshape(2, P).T
    biases[:, 6] = x["ob3"]
    biases[0:D, 7] = x["db1"]
    biases[0:D, 8] = x["db2"]
    biases[0, 9] = x["ob4"][0]
    base = _np.tile(_np.arange(NF, dtype=_np.int32) * V, (P, TILES))

    arrays = {
        "dense_t_dram": x["r_dense"].T,
        "idx_dram": idx,
        "first_dram": _np.stack([base, idx[:, 0]], axis=1),
        "table_dram": x["emb_tables"].reshape(NF * V, D),
        "dw1_dram": x["dw1"],
        "dw2_dram": x["dw2"],
        "ow1_dram": x["ow1"],
        "ow1_pairs_dram": ow1_pairs,
        "ow2_dram": x["ow2"],
        "ow3_dram": x["ow3"],
        "ow4_dram": x["ow4"],
        "biases_dram": biases,
        "ident_dram": _np.eye(P, dtype=_np.float32),
    }
    arrays = {k: _np.ascontiguousarray(v) for k, v in arrays.items()}
    nc = _bacc.Bacc("TRN2", target_bir_lowering=False, num_devices=1)
    args = [nc.dram_tensor(k, a.shape, _mybir.dt.from_np(a.dtype), kind="ExternalInput").ap()
            for k, a in arrays.items()]
    args.append(nc.dram_tensor("out_dram", (B, 1), F32, kind="ExternalOutput").ap())
    bass_dlrm_kernel(nc, *args, V)
    r = _run(nc, [arrays], core_ids=[0])
    return r.results[0]["out_dram"]
```
